# Optimizing a Trainium2 kernel written in Bass

```python
import numpy as np
import jax
import jax.numpy as jnp

def _softmax(x, axis=-1):
    return jax.nn.softmax(x, axis=axis)

def _gelu(x):
    return jax.nn.gelu(x, approximate=True)

def _silu(x):
    return jax.nn.silu(x)

def _sigmoid(x):
    return jax.nn.sigmoid(x)

def _layernorm(x, axis=-1, eps=1e-05):
    m = jnp.mean(x, axis=axis, keepdims=True)
    v = jnp.var(x, axis=axis, keepdims=True)
    return (x - m) / jnp.sqrt(v + eps)

def _scatter_add(tgt, idx, src, axis=0):
    return tgt.at[idx].add(src)

def _segment_sum(src, seg, n):
    return jax.ops.segment_sum(src, seg, n)
kernel_name = 'mk_adaln_attn_ffn_d1_seqx_r8_1ab20b'

def setup_inputs(seed: int=0):
    np.random.seed(seed)
    _w = jnp.asarray

    def _rec_inputs():
        import jax
        import jax.numpy as jnp
        _rk = jax.random.key(seed)
        x = -7.109e-05 + 0.9999 * jax.random.normal(jax.random.fold_in(_rk, 1), (128, 32, 256), jnp.float32)
        _lenS = 32 - jax.random.randint(jax.random.fold_in(_rk, 7), (128,), 0, max(1, 32 // 4) + 1, jnp.int32)
        _lenS2 = 32 - jax.random.randint(jax.random.fold_in(_rk, 8), (128,), 0, max(1, 32 // 4) + 1, jnp.int32)
        itok_B_1_198 = jax.random.randint(jax.random.fold_in(_rk, 11), (128,), 1, 199, jnp.int32)
        itok_B_0_6 = jax.random.randint(jax.random.fold_in(_rk, 12), (128,), 0, 7, jnp.int32)
        return (x, itok_B_1_198, itok_B_0_6)
    x, itok_B_1_198, itok_B_0_6 = _rec_inputs()

    def _L0_cond_setup():
        import jax, jax.numpy as jnp
        import numpy as np
        B, C, T = (128, 32, 256)
        S, D = (200, 32)
        key = jax.random.key(seed)
        k1, k2, k3 = jax.random.split(key, 3)
        x = jax.random.normal(k1, (B, C, T), dtype=jnp.float32)
        conditions = jax.random.randint(k2, (B,), 0, S, dtype=jnp.int64)
        weights = jax.random.normal(k3, (S, C, D), dtype=jnp.float32) / jnp.sqrt(jnp.float32(C))
        return {'x': x, 'conditions': conditions, 'weights': weights}
    _L0_cond_all = _L0_cond_setup()
    _L0_cond_in = {k: v for k, v in _L0_cond_all.items() if k in ('weights',)}
    del _L0_cond_all

    def _L0_attn_setup():
        import jax, jax.numpy as jnp
        import numpy as np
        B, L, D, H = (4, 512, 256, 16)
        HD = D // H
        EPS = 1e-09

        def phi(x):
            return jax.nn.elu(x) + 1.0
        key = jax.random.key(seed)
        k1, k2, k3 = jax.random.split(key, 3)
        x = jax.random.normal(k1, (B, L, D), dtype=jnp.float32)
        W_qkv = jax.random.normal(k2, (3 * D, D), dtype=jnp.float32) * D ** (-0.5)
        W_out = jax.random.normal(k3, (D, D), dtype=jnp.float32) * D ** (-0.5)
        return {'x': x, 'W_qkv': W_qkv, 'W_out': W_out}
    _L0_attn_all = _L0_attn_setup()
    _L0_attn_in = {k: v for k, v in _L0_attn_all.items() if k in ('W_qkv', 'W_out')}
    del _L0_attn_all

    def _L0_cond2_setup():
        import jax, jax.numpy as jnp
        import numpy as np
        B, T, D_IN, D_OUT = (16, 256, 256, 256)
        N_ADAPTERS, RANK = (8, 16)
        key = jax.random.key(seed)
        k_x, k_w, k_a, k_b, k_s, k_idx = jax.random.split(key, 6)
        x = jax.random.normal(k_x, (B, T, D_IN), dtype=jnp.float32)
        W = jax.random.normal(k_w, (D_OUT, D_IN), dtype=jnp.float32) * (1.0 / np.sqrt(D_IN))
        A = jax.random.normal(k_a, (N_ADAPTERS, RANK, D_IN), dtype=jnp.float32) * 0.02
        Bm = jax.random.normal(k_b, (N_ADAPTERS, D_OUT, RANK), dtype=jnp.float32) * 0.02
        scalings = jnp.ones((N_ADAPTERS,), dtype=jnp.float32)
        adapter_idx = jax.random.randint(k_idx, (B,), 0, N_ADAPTERS, dtype=jnp.int32)
        return {'x': x, 'W': W, 'A': A, 'Bm': Bm, 'scalings': scalings, 'adapter_idx': adapter_idx}
    _L0_cond2_all = _L0_cond2_setup()
    _L0_cond2_in = {k: v for k, v in _L0_cond2_all.items() if k in ('W', 'A', 'Bm', 'scalings')}
    del _L0_cond2_all

    def _L0_ffn_setup():
        import jax, jax.numpy as jnp
        import numpy as np

        def _sparsify_2to4(h):
            B, S, I = h.shape
            g = h.reshape(B, S, I // 4, 4)
            a = jnp.abs(g)
            _, idx = jax.lax.top_k(a, 2)
            pos = jnp.arange(4)
            mask = (pos == idx[..., 0:1]) | (pos == idx[..., 1:2])
            return (g * mask.astype(g.dtype)).reshape(B, S, I)
        key = jax.random.key(seed)
        k1, k2, k3, k4 = jax.random.split(key, 4)
        B, S, H, I = (4, 256, 256, 1024)
        x = jax.random.normal(k1, (B, S, H), dtype=jnp.float32)
        w_gate = jax.random.normal(k2, (H, I), dtype=jnp.float32) / np.sqrt(H)
        w_up = jax.random.normal(k3, (H, I), dtype=jnp.float32) / np.sqrt(H)
        w_down = jax.random.normal(k4, (I, H), dtype=jnp.float32) / np.sqrt(I)
        return {'x': x, 'w_gate': w_gate, 'w_up': w_up, 'w_down': w_down}
    _L0_ffn_all = _L0_ffn_setup()
    _L0_ffn_in = {k: v for k, v in _L0_ffn_all.items() if k in ('w_gate', 'w_up', 'w_down')}
    del _L0_ffn_all
    return {'x': x, 'itok_B_1_198': itok_B_1_198, 'itok_B_0_6': itok_B_0_6, 'L0_cond_weights': _L0_cond_in['weights'], 'L0_attn_W_qkv': _L0_attn_in['W_qkv'], 'L0_attn_W_out': _L0_attn_in['W_out'], 'L0_cond2_W': _L0_cond2_in['W'], 'L0_cond2_A': _L0_cond2_in['A'], 'L0_cond2_Bm': _L0_cond2_in['Bm'], 'L0_cond2_scalings': _L0_cond2_in['scalings'], 'L0_ffn_w_gate': _L0_ffn_in['w_gate'], 'L0_ffn_w_up': _L0_ffn_in['w_up'], 'L0_ffn_w_down': _L0_ffn_in['w_down']}

def reference(x, itok_B_1_198, itok_B_0_6, L0_cond_weights, L0_attn_W_qkv, L0_attn_W_out, L0_cond2_W, L0_cond2_A, L0_cond2_Bm, L0_cond2_scalings, L0_ffn_w_gate, L0_ffn_w_up, L0_ffn_w_down):
    import jax
    import jax.numpy as jnp

    def _L0_cond_ref(x, conditions, weights):
        import jax, jax.numpy as jnp
        import numpy as np
        B, C, T = (128, 32, 256)
        S, D = (200, 32)
        w = weights[conditions]
        return jnp.einsum('bct,bcd->bdt', x, w)

    def _L0_attn_ref(x, W_qkv, W_out):
        import jax, jax.numpy as jnp
        import numpy as np
        B, L, D, H = (4, 512, 256, 16)
        HD = D // H
        EPS = 1e-09

        def phi(x):
            return jax.nn.elu(x) + 1.0
        b, l, d = x.shape
        qkv = x @ W_qkv.T
        q, k, v = jnp.split(qkv, 3, axis=-1)
        q = q.reshape(b, l, H, HD).transpose(0, 2, 1, 3)
        k = k.reshape(b, l, H, HD).transpose(0, 2, 1, 3)
        v = v.reshape(b, l, H, HD).transpose(0, 2, 1, 3)
        q = phi(q)
        k = phi(k)
        kv_cumsum = jnp.cumsum(k * v, axis=2)
        k_cumsum = jnp.cumsum(k, axis=2)
        out = q * kv_cumsum / (q * k_cumsum + EPS)
        out = out.transpose(0, 2, 1, 3).reshape(b, l, d)
        return out @ W_out.T * HD ** (-0.5)

    def _L0_cond2_ref(x, W, A, Bm, scalings, adapter_idx):
        import jax, jax.numpy as jnp
        import numpy as np
        B, T, D_IN, D_OUT = (16, 256, 256, 256)
        N_ADAPTERS, RANK = (8, 16)
        H = jnp.einsum('btd,od->bto', x, W)
        A_b = A[adapter_idx]
        B_b = Bm[adapter_idx]
        s_b = scalings[adapter_idx]
        xa = jnp.einsum('btd,brd->btr', x, A_b)
        delta = jnp.einsum('btr,bor->bto', xa, B_b)
        delta = jax.lax.stop_gradient(delta * s_b[:, None, None])
        return H + delta

    def _L0_ffn_ref(x, w_gate, w_up, w_down):
        import jax, jax.numpy as jnp
        import numpy as np

        def _sparsify_2to4(h):
            B, S, I = h.shape
            g = h.reshape(B, S, I // 4, 4)
            a = jnp.abs(g)
            _, idx = jax.lax.top_k(a, 2)
            pos = jnp.arange(4)
            mask = (pos == idx[..., 0:1]) | (pos == idx[..., 1:2])
            return (g * mask.astype(g.dtype)).reshape(B, S, I)
        h = jax.nn.silu(jnp.einsum('bsh,hi->bsi', x, w_gate)) * jnp.einsum('bsh,hi->bsi', x, w_up)
        h_sparse = _sparsify_2to4(h)
        return jnp.einsum('bsi,ih->bsh', h_sparse, w_down)
    x = x + _L0_attn_ref(_L0_cond_ref(x, itok_B_1_198, L0_cond_weights), L0_attn_W_qkv, L0_attn_W_out)
    x = x + _L0_ffn_ref(_L0_cond2_ref(x, L0_cond2_W, L0_cond2_A, L0_cond2_Bm, L0_cond2_scalings, itok_B_0_6), L0_ffn_w_gate, L0_ffn_w_up, L0_ffn_w_down)
    return x

_drawn_inputs = setup_inputs


def setup_inputs(seed=0):
    import zlib

    import numpy as np

    out = dict(_drawn_inputs(seed))
    spreads = {'L0_cond2_scalings': (1.0, 0.2)}
    factors = {}
    for name, (base, spread) in spreads.items():
        noise = np.random.default_rng([zlib.crc32(name.encode()), seed]).standard_normal(out[name].shape)
        drawn = base * np.exp(spread * noise) if base else spread * noise
        out[name] = jnp.asarray(drawn.astype(out[name].dtype))
    for name, factor in factors.items():
        out[name] = (out[name] * factor).astype(out[name].dtype)
    return out
```

```python
from contextlib import ExitStack

import concourse.bass as bass
from concourse import mybir

F32 = mybir.dt.float32
F32R = mybir.dt.float32r
BF16 = mybir.dt.bfloat16
I32 = mybir.dt.int32
U32 = mybir.dt.uint32
ALU = mybir.AluOpType
ACT = mybir.ActivationFunctionType

P = 128
ATTN_EPS = 1e-09


def adaln_attn_ffn(
    nc: bass.Bass,
    x_rows: bass.AP,
    x_cols: bass.AP,
    cond_idx: bass.AP,
    adapter_idx: bass.AP,
    cond_w: bass.AP,
    w_qkv: bass.AP,
    w_out: bass.AP,
    w_ada: bass.AP,
    lora_a: bass.AP,
    lora_b: bass.AP,
    lora_scale: bass.AP,
    lora_id: bass.AP,
    w_gate: bass.AP,
    w_up: bass.AP,
    w_down: bass.AP,
    y_cols: bass.AP,
):
    ROWS, T = x_rows.shape
    B = cond_idx.shape[0]
    C = ROWS // B
    NT = 512
    TILES = ROWS // NT
    KH = T // P
    GRP = NT // P
    BPG = P // C
    BPT = NT // C
    MEMB = w_gate.shape[1]
    QB = w_gate.shape[2] // P
    NB = QB * MEMB
    HEAD_SCALE = 16 ** -0.5
    STEPS = 6
    assert KH == 2 and MEMB == 4 and QB == 2 and lora_b.shape[0] == P and B == P

    FRONT = ["cond0", "cond1", "q0", "k0", "q1", "k1", "v0", "v1", "out0", "out1", "xa", "ada0", "ada1"]
    BANK = {"cond0": 0, "cond1": 1, "q0": 0, "k0": 1, "q1": 0, "k1": 1, "v0": 0, "v1": 1,
            "out0": 0, "out1": 1, "xa": 0, "ada0": 1, "ada1": 0}
    FREED = ["cond0", "cond1", "v0", "v1", "out0", "out1", "xa", "ada0", "ada1"]
    NF, NV = len(FRONT), len(FREED)

    def made(t, name):
        return NF * t + FRONT.index(name) + 1

    def freed(t, name):
        return NV * t + FREED.index(name) + 1

    ctx = ExitStack()
    with ctx:
        def sb(name, shape, dt=F32):
            return ctx.enter_context(nc.sbuf_tensor(name, shape, dt))

        def bank(name):
            return ctx.enter_context(nc.psum_tensor(name, [P, NT], F32))

        def sem(name):
            return ctx.enter_context(nc.semaphore(name))

        qkv_hi, qkv_lo = (sb(f"qkv_{s}", [P, KH, 3 * T], F32R) for s in ("hi", "lo"))
        wo_hi, wo_lo = (sb(f"wo_{s}", [P, KH, T], F32R) for s in ("hi", "lo"))
        wa_hi, wa_lo = (sb(f"wa_{s}", [P, KH, T], F32R) for s in ("hi", "lo"))
        la_hi, la_lo = (sb(f"la_{s}", [P, KH, P], F32R) for s in ("hi", "lo"))
        lb_hi, lb_lo = (sb(f"lb_{s}", [P, T], F32R) for s in ("hi", "lo"))
        gate_hi, gate_lo = (sb(f"gate_{s}", [P, KH, MEMB, QB * P], F32R) for s in ("hi", "lo"))
        up_hi, up_lo = (sb(f"up_{s}", [P, KH, MEMB, QB * P], F32R) for s in ("hi", "lo"))
        wd_hi, wd_lo = (sb(f"wd_{s}", [P, QB, MEMB, T], F32R) for s in ("hi", "lo"))
        hid = sb("hid", [P, QB, MEMB, NT])
        mag = sb("mag", [P, QB, MEMB, NT])
        sparse_hi, sparse_lo = (sb(f"sparse_{s}", [P, MEMB, NT], F32R) for s in ("hi", "lo"))
        raw_gate = hid[:, 0].rearrange("p j n -> p (j n)").rearrange("p (h j q) -> p h j q", h=KH, j=MEMB)
        raw_up = hid[:, 1].rearrange("p j n -> p (j n)").rearrange("p (h j q) -> p h j q", h=KH, j=MEMB)
        raw_s = mag[:, :].rearrange("p m j n -> p (m j n)")
        at = 0
        raws = []
        for n in (KH * 3 * T, KH * T, KH * T, KH * P, T):
            raws.append(raw_s[:, at:at + n])
            at += n
        raw_qkv, raw_wo, raw_wa, raw_la = (r.rearrange("p (h n) -> p h n", h=KH) for r in raws[:4])
        raw_lb = raws[4]
        y = sb("y", [P, KH, NT])
        raw_wd = [r.rearrange("p (j n) -> p j n", j=MEMB)
                  for r in (raw_s[:, at:at + MEMB * T], y[:].rearrange("p h n -> p (h n)"))]

        xrow = sb("xrow", [P, GRP, T])
        bdiag = sb("bdiag", [P, GRP, P])
        xcol = sb("xcol", [P, KH, NT])
        xc_hi, xc_lo = (sb(f"xc_{s}", [P, KH, NT], F32R) for s in ("hi", "lo"))
        expo = sb("expo", [P, 2, NT])
        phi = sb("phi", [P, 4, NT])
        kvs = sb("kvs", [P, KH, NT])
        kcs = sb("kcs", [P, KH, NT])
        guess = expo
        eps = sb("eps", [P, 1])
        x1 = sb("x1", [P, KH, NT])
        x1_hi, x1_lo = (sb(f"x1_{s}", [P, KH, NT], F32R) for s in ("hi", "lo"))
        xa = sb("xa", [P, NT])
        xa_hi, xa_lo = (sb(f"xa_{s}", [P, NT], F32R) for s in ("hi", "lo"))
        h2_hi, h2_lo = (sb(f"h2_{s}", [P, KH, NT], F32R) for s in ("hi", "lo"))
        silu = sb("silu", [P, 2, NT])
        beats = sb("beats", [P, 2, 2, NT], BF16)
        inner = sb("inner", [P, 2, NT], BF16)
        wins = sb("wins", [P, NT], BF16)
        x1_held = sb("x1_held", [P, KH, NT])
        carry = sb("carry", [P, NT])
        cidx = sb("cidx", [P, 1], I32)
        aidx = sb("aidx", [P, B], I32)
        lscale = sb("lscale", [P, 1])
        lid = sb("lid", [P, 1])
        lmask = sb("lmask", [P, B])
        gathered = hid[:, 0].rearrange("p j n -> p (j n)")[:, 0:C * C]
        w_sel = nc.dram_tensor("w_sel", (B, C * C), F32).ap()

        gate_ps = [bank(f"gate_ps{n}") for n in range(2)]
        up_ps = [bank(f"up_ps{n}") for n in range(2)]
        down_ps = [bank(f"down_ps{n}") for n in range(KH)]
        front_ps = [bank(f"front_ps{n}") for n in range(2)]

        idx_in = sem("idx_in")
        gather_in = sem("gather_in")
        gather_out = sem("gather_out")
        bdiag_zero = sem("bdiag_zero")
        tables_in = sem("tables_in")
        qkv_in, wproj_in, gate_in, up_in, wd_in = (sem(f"{n}_in") for n in ("qkv", "wproj", "gate", "up", "wd"))
        w_hi_ready = sem("w_hi_ready")
        w_ready = sem("w_ready")
        tables_ready = sem("tables_ready")
        mask_ready = sem("mask_ready")
        xrow_in, bdiag_in, xcol_in = sem("xrow_in"), sem("bdiag_in"), sem("xcol_in")
        front_made = sem("front_made")
        front_freed = sem("front_freed")
        phi_parts = sem("phi_parts")
        phi_made = sem("phi_made")
        xc_hi_made, at_hi_made, x1_hi_made, xa_hi_made, h2_hi_made = (
            sem(f"{n}_hi_made") for n in ("xc", "at", "x1", "xa", "h2"))
        attn_step = [sem(f"attn_step{d}") for d in range(KH)]
        ln_made, guess_made, at_made = sem("ln_made"), sem("guess_made"), sem("at_made")
        at_ready, x1_ready, xa_ready = sem("at_ready"), sem("x1_ready"), sem("xa_ready")
        gu_made = sem("gu_made")
        silu_made = sem("silu_made")
        hid_made = sem("hid_made")
        mag_made = sem("mag_made")
        sel_step = sem("sel_step")
        sparse_made = sem("sparse_made")
        sparse_hi_made = sem("sparse_hi_made")
        sparse_ready = sem("sparse_ready")
        down_made = sem("down_made")
        y_made = sem("y_made")
        y_stored = sem("y_stored")
        held = sem("held")

        SPLITS = [
            (raw_qkv[:, 0], qkv_hi[:, 0], qkv_lo[:, 0], qkv_in, 16),
            (raw_qkv[:, 1], qkv_hi[:, 1], qkv_lo[:, 1], qkv_in, 16),
            (raw_wo, wo_hi, wo_lo, wproj_in, 64),
            (raw_wa, wa_hi, wa_lo, wproj_in, 64),
            (raw_la, la_hi, la_lo, wproj_in, 64),
            (raw_lb, lb_hi, lb_lo, wproj_in, 64),
            (raw_gate[:, 0], gate_hi[:, 0], gate_lo[:, 0], gate_in, 16),
            (raw_gate[:, 1], gate_hi[:, 1], gate_lo[:, 1], gate_in, 16),
            (raw_up[:, 0], up_hi[:, 0], up_lo[:, 0], up_in, 16),
            (raw_up[:, 1], up_hi[:, 1], up_lo[:, 1], up_in, 16),
            (raw_wd[0], wd_hi[:, 0], wd_lo[:, 0], wd_in, 32),
            (raw_wd[1], wd_hi[:, 1], wd_lo[:, 1], wd_in, 32),
        ]
        QKV_SPLIT, PROJ_SPLIT, ALL_SPLIT = 2, 6, len(SPLITS)

        block = ctx.enter_context(nc.Block())

        @block.sync
        def _(sp):
            xrow_v = x_rows.rearrange("(n g p) t -> n p g t", g=GRP, p=P)
            xcol_v = x_cols.rearrange("(h p) (n r) -> n p h r", p=P, r=NT)
            wsel_v = w_sel.rearrange("(n g j) (c d) -> n j c g d", g=GRP, j=BPG, c=C)
            y_v = y_cols.rearrange("(h p) (n r) -> n p h r", p=P, r=NT)

            def load_front(t):
                if not (isinstance(t, int) and t == 0):
                    sp.wait_ge(front_made, made(t - 1, "cond1"))
                sp.dma_start(xrow[:], xrow_v[t]).then_inc(xrow_in, 16)
                for j in range(BPG):
                    sp.dma_start(bdiag[C * j:C * (j + 1), :, C * j:C * (j + 1)], wsel_v[t, j]).then_inc(bdiag_in, 16)

            def load_xcol(t, stored=None):
                if not (isinstance(t, int) and t == 0):
                    taken = freed(t - 1, "out1")
                    if stored is not None:
                        taken, stored = sp.snap(taken), sp.snap(16 * stored)
                        sp.wait_ge(y_stored, stored)
                    sp.wait_ge(front_freed, taken)
                sp.dma_start(xcol[:], xcol_v[t]).then_inc(xcol_in, 16)

            def store(i):
                sp.wait_ge(y_made, KH * (i + 1))
                sp.dma_start(y_v[i], y[:]).then_inc(y_stored, 16)

            sp.dma_start(cidx[:], cond_idx).then_inc(idx_in, 16)
            sp.dma_start(xrow[:], xrow_v[0]).then_inc(xrow_in, 16)
            sp.dma_start(raw_qkv, w_qkv.rearrange("(h p) n -> p h n", p=P)).then_inc(qkv_in, 16)
            sp.wait_ge(gather_in, 16)
            sp.dma_start(w_sel, gathered).then_inc(gather_out, 16)
            sp.wait_ge(gather_out, 16)
            sp.wait_ge(bdiag_zero, 1)
            for j in range(BPG):
                sp.dma_start(bdiag[C * j:C * (j + 1), :, C * j:C * (j + 1)], wsel_v[0, j]).then_inc(bdiag_in, 16)
            load_xcol(0)
            sp.dma_start(raw_gate, w_gate.rearrange("(h p) j q -> p h j q", p=P)).then_inc(gate_in, 16)
            sp.dma_start(raw_up, w_up.rearrange("(h p) j q -> p h j q", p=P)).then_inc(up_in, 16)
            for m in range(QB):
                sp.dma_start(raw_wd[m], w_down[P * m:P * (m + 1)].rearrange("p (j n) -> p j n", j=MEMB)).then_inc(wd_in, 16)
            load_front(1)
            load_xcol(1)
            with sp.Fori(1, TILES - 1) as i:
                load_front(i + 1)
                store(i - 1)
                load_xcol(i + 1, stored=i)
            store(TILES - 2)
            store(TILES - 1)
            sp.wait_ge(y_stored, 16 * TILES)

        @block.gpsimd
        def _(pool):
            nc.gpsimd.memset(bdiag[:], 0.0).then_inc(bdiag_zero, 1)
            pool.wait_ge(idx_in, 16)
            nc.gpsimd.indirect_dma_start(
                out=gathered, out_offset=None, in_=cond_w,
                in_offset=bass.IndirectOffsetOnAxis(ap=cidx[:, 0:1].bitcast(U32), axis=0)).then_inc(gather_in, 16)
            nc.gpsimd.memset(eps[:], ATTN_EPS).then_inc(tables_ready, 1)
            nc.gpsimd.memset(carry[:], 1.0).then_inc(tables_ready, 1)
            pool.wait_ge(tables_ready, 2)
            nc.gpsimd.memset(carry[:].rearrange("p (b l) -> p b l", l=C)[:, :, 0:1], 0.0).then_inc(tables_ready, 1)

        @block.tensor
        def _(pe):
            def split_product(ps, terms, start=True, stop=True):
                for n, (w_hi, w_lo, v_hi, v_lo) in enumerate(terms):
                    nc.tensor.matmul(ps, w_hi, v_lo, start=start and n == 0, stop=False)
                    nc.tensor.matmul(ps, w_lo, v_hi, start=False, stop=False)
                    last = nc.tensor.matmul(ps, w_hi, v_hi, start=False, stop=stop and n == len(terms) - 1)
                return last

            def cond(t):
                pe.wait_ge(xrow_in, 16 * (t + 1))
                pe.wait_ge(bdiag_in, 16 * BPG * (t + 1))
                if not (isinstance(t, int) and t == 0):
                    pe.wait_ge(front_freed, freed(t - 1, "ada1"))
                for h in range(KH):
                    for g in range(GRP):
                        last = nc.tensor.matmul(front_ps[h][:, P * g:P * (g + 1)], xrow[:, g, P * h:P * (h + 1)],
                                                bdiag[:, g, :], start=True, stop=True)
                    last.then_inc(front_made, 1)

            def project(part, d):
                col = T * part + P * d
                bnk = BANK["qkv"[part] + str(d)]
                split_product(front_ps[bnk][:], [
                    (qkv_hi[:, k, col:col + P], qkv_lo[:, k, col:col + P], xc_hi[:, k], xc_lo[:, k])
                    for k in range(KH)]).then_inc(front_made, 1)

            def qk(t):
                pe.wait_ge(front_freed, freed(t, "cond1"))
                project(0, 0)
                project(1, 0)
                pe.wait_ge(phi_parts, 4 * t + 1)
                project(0, 1)
                pe.wait_ge(phi_parts, 4 * t + 2)
                project(1, 1)

            def v(t):
                pe.wait_ge(phi_parts, 4 * t + 3)
                project(2, 0)
                pe.wait_ge(phi_parts, 4 * t + 4)
                project(2, 1)

            def out_proj(t):
                pe.wait_ge(at_ready, KH * (t + 1))
                for h in range(KH):
                    split_product(front_ps[BANK[f"out{h}"]][:], [
                        (wo_hi[:, k, P * h:P * (h + 1)], wo_lo[:, k, P * h:P * (h + 1)], xc_hi[:, k], xc_lo[:, k])
                        for k in range(KH)]).then_inc(front_made, 1)

            def lora_in(t):
                pe.wait_ge(x1_ready, KH * (t + 1))
                split_product(front_ps[BANK["xa"]][:], [
                    (la_hi[:, k], la_lo[:, k], x1_hi[:, k], x1_lo[:, k]) for k in range(KH)]).then_inc(front_made, 1)

            def adapted(t):
                for h in range(KH):
                    cols = slice(P * h, P * (h + 1))
                    ps = front_ps[BANK[f"ada{h}"]][:]
                    if h:
                        pe.wait_ge(xa_ready, t + 1)
                    split_product(ps, [(wa_hi[:, k, cols], wa_lo[:, k, cols], x1_hi[:, k], x1_lo[:, k])
                                       for k in range(KH)], stop=False)
                    if not h:
                        pe.wait_ge(xa_ready, t + 1)
                    split_product(ps, [(lb_hi[:, cols], lb_lo[:, cols], xa_hi[:], xa_lo[:])],
                                  start=False).then_inc(front_made, 1)

            def gate_up(i, b, first=False):
                m, j = divmod(b, MEMB)
                cols = slice(P * m, P * (m + 1))
                if not (first and b < 2):
                    pe.wait_ge(silu_made, NB * i + b - 1)
                split_product(gate_ps[b % 2][:], [
                    (gate_hi[:, k, j, cols], gate_lo[:, k, j, cols], h2_hi[:, k], h2_lo[:, k])
                    for k in range(KH)]).then_inc(gu_made, 1)
                if not (first and b < 2):
                    pe.wait_ge(hid_made, NB * i + b - 1)
                split_product(up_ps[b % 2][:], [
                    (up_hi[:, k, j, cols], up_lo[:, k, j, cols], h2_hi[:, k], h2_lo[:, k])
                    for k in range(KH)]).then_inc(gu_made, 1)

            def down(i, m):
                if m == 0:
                    pe.wait_ge(held, i + 1)
                for j in range(MEMB):
                    pe.wait_ge(sparse_ready, NB * i + MEMB * m + j + 1)
                    for h in range(KH):
                        cols = slice(P * h, P * (h + 1))
                        last = split_product(
                            down_ps[h][:], [(wd_hi[:, m, j, cols], wd_lo[:, m, j, cols], sparse_hi[:, j], sparse_lo[:, j])],
                            start=(m == 0 and j == 0), stop=(m == QB - 1 and j == MEMB - 1))
                    last.then_inc(down_made, 1)

            def step(i, first=False, last=False):
                if not last:
                    cond(i + 1)
                pe.wait_ge(front_freed, freed(i, "ada1"))
                gate_up(i, 0, first)
                if not last:
                    qk(i + 1)
                if not first:
                    down(i - 1, 0)
                if not last:
                    v(i + 1)
                gate_up(i, 1, first)
                if not first:
                    down(i - 1, 1)
                gate_up(i, 2, first)
                gate_up(i, 3, first)
                gate_up(i, 4, first)
                gate_up(i, 5, first)
                if not last:
                    out_proj(i + 1)
                gate_up(i, 6, first)
                if not last:
                    lora_in(i + 1)
                gate_up(i, 7, first)
                if not last:
                    adapted(i + 1)

            cond(0)
            pe.wait_ge(w_ready, QKV_SPLIT)
            qk(0)
            v(0)
            pe.wait_ge(w_ready, PROJ_SPLIT)
            out_proj(0)
            lora_in(0)
            adapted(0)
            pe.wait_ge(w_ready, ALL_SPLIT)
            step(0, first=True)
            with pe.Fori(1, TILES - 1) as i:
                step(i)
            step(TILES - 1, last=True)
            down(TILES - 1, 0)
            down(TILES - 1, 1)

        @block.scalar
        def _(act):
            def exp_ln_set():
                nc.scalar.preload_act_table_set("natural_log_exp_and_others")

            def silu_set():
                nc.scalar.preload_act_table_set("silu_and_others")

            def split_weight(n):
                raw, hi, _, arrived, count = SPLITS[n]
                act.wait_ge(arrived, count)
                nc.scalar.copy(hi[:] if len(hi.shape) < 3 else hi[:, :], raw).then_inc(w_hi_ready, 1)

            def cond_hi(t):
                for h in range(KH):
                    act.wait_ge(front_made, made(t, f"cond{h}"))
                    nc.scalar.copy(xc_hi[:, h], front_ps[h][:]).then_inc(xc_hi_made, 1)

            def phi_terms(t, s):
                ps = front_ps[s % 2][:]
                act.wait_ge(front_made, made(t, FRONT[2 + s]))
                if s >= 2:
                    act.wait_ge(phi_made, 4 * t + s - 1)
                elif not (isinstance(t, int) and t == 0):
                    act.wait_ge(phi_made, 4 * t + s - 1)
                if s == 0 and not (isinstance(t, int) and t == 0):
                    act.wait_ge(at_ready, KH * t)
                nc.scalar.activation(expo[:, s % 2], ps, ACT.Exp)
                nc.scalar.activation(phi[:, s], ps, ACT.Relu).then_inc(phi_parts, 1)

            def guess_inverse(t, d):
                act.wait_ge(attn_step[d], STEPS * t + 3)
                if d == 0:
                    act.wait_ge(phi_made, 4 * (t + 1))
                nc.scalar.activation(guess[:, d], kcs[:, d], ACT.Ln, bias=eps[:]).then_inc(ln_made, 1)
                act.wait_ge(ln_made, KH * t + d + 1)
                nc.scalar.activation(guess[:, d], guess[:, d], ACT.Exp, scale=-1.0).then_inc(guess_made, 1)

            def attn_hi(t, d):
                act.wait_ge(at_made, KH * t + d + 1)
                act.wait_ge(front_made, made(t, "v1"))
                nc.scalar.copy(xc_hi[:, d], kvs[:, d]).then_inc(at_hi_made, 1)

            def x1_hi_part(t, h):
                act.wait_ge(front_freed, freed(t, f"out{h}"))
                nc.scalar.copy(x1_hi[:, h], x1[:, h]).then_inc(x1_hi_made, 1)

            def xa_hi_part(t):
                act.wait_ge(front_freed, freed(t, "xa"))
                nc.scalar.copy(xa_hi[:], xa[:]).then_inc(xa_hi_made, 1)

            def h2_hi_part(t, h):
                act.wait_ge(front_made, made(t, f"ada{h}"))
                nc.scalar.copy(h2_hi[:, h], front_ps[BANK[f"ada{h}"]][:]).then_inc(h2_hi_made, 1)

            def silu_gate(i, b, first=False):
                act.wait_ge(gu_made, 2 * (NB * i + b) + 1)
                if not (first and b < 2):
                    act.wait_ge(hid_made, NB * i + b - 1)
                nc.scalar.activation(silu[:, b % 2], gate_ps[b % 2][:], ACT.Silu).then_inc(silu_made, 1)

            def magnitude(i, b):
                m, j = divmod(b, MEMB)
                act.wait_ge(hid_made, NB * i + b + 1)
                nc.scalar.activation(mag[:, m, j], hid[:, m, j], ACT.Abs).then_inc(mag_made, 1)

            def sparse_hi_part(i, m, a):
                act.wait_ge(sparse_made, NB * i + MEMB * m + 2 * (a + 1))
                if m:
                    act.wait_ge(down_made, NB * i + 2 * (a + 1))
                nc.scalar.copy(sparse_hi[:, 2 * a:2 * (a + 1)], hid[:, m, 2 * a:2 * (a + 1)]).then_inc(sparse_hi_made, 1)

            def hold_x1(i):
                if not (isinstance(i, int) and i == 0):
                    act.wait_ge(y_made, KH * i)
                nc.scalar.copy(x1_held[:], x1[:]).then_inc(held, 1)

            def step(i, first=False, last=False):
                t = i + 1
                if not last:
                    cond_hi(t)
                if not first:
                    sparse_hi_part(i - 1, 0, 0)
                silu_gate(i, 0, first)
                if not last:
                    exp_ln_set()
                    phi_terms(t, 0)
                    phi_terms(t, 1)
                if not first:
                    sparse_hi_part(i - 1, 0, 1)
                if not last:
                    phi_terms(t, 2)
                    phi_terms(t, 3)
                if not first:
                    sparse_hi_part(i - 1, 1, 0)
                    sparse_hi_part(i - 1, 1, 1)
                magnitude(i, 0)
                if not last:
                    silu_set()
                silu_gate(i, 1, first)
                if not last:
                    exp_ln_set()
                    guess_inverse(t, 0)
                    guess_inverse(t, 1)
                    silu_set()
                silu_gate(i, 2, first)
                magnitude(i, 1)
                silu_gate(i, 3, first)
                magnitude(i, 2)
                if not last:
                    attn_hi(t, 0)
                hold_x1(i)
                if not last:
                    attn_hi(t, 1)
                magnitude(i, 3)
                silu_gate(i, 4, first)
                silu_gate(i, 5, first)
                if not last:
                    x1_hi_part(t, 0)
                    x1_hi_part(t, 1)
                    xa_hi_part(t)
                silu_gate(i, 6, first)
                silu_gate(i, 7, first)
                magnitude(i, 4)
                magnitude(i, 5)
                magnitude(i, 6)
                magnitude(i, 7)
                if not last:
                    h2_hi_part(t, 0)
                    h2_hi_part(t, 1)

            act.dma_start(raw_wo, w_out.rearrange("(h p) n -> p h n", p=P)).then_inc(wproj_in, 16)
            act.dma_start(raw_wa, w_ada.rearrange("(h p) n -> p h n", p=P)).then_inc(wproj_in, 16)
            act.dma_start(raw_la, lora_a.rearrange("(h p) n -> p h n", p=P)).then_inc(wproj_in, 16)
            act.dma_start(raw_lb, lora_b).then_inc(wproj_in, 16)
            act.dma_start(aidx[:], adapter_idx.to_broadcast([P, B])).then_inc(tables_in, 16)
            act.dma_start(lscale[:], lora_scale).then_inc(tables_in, 16)
            act.dma_start(lid[:], lora_id).then_inc(tables_in, 16)
            exp_ln_set()
            for n in range(PROJ_SPLIT):
                split_weight(n)
            cond_hi(0)
            for s in range(4):
                phi_terms(0, s)
            act.wait_ge(tables_ready, 3)
            guess_inverse(0, 0)
            guess_inverse(0, 1)
            silu_set()
            for n in range(PROJ_SPLIT, ALL_SPLIT):
                split_weight(n)
            attn_hi(0, 0)
            attn_hi(0, 1)
            x1_hi_part(0, 0)
            x1_hi_part(0, 1)
            xa_hi_part(0)
            h2_hi_part(0, 0)
            h2_hi_part(0, 1)
            step(0, first=True)
            with act.Fori(1, TILES - 1) as i:
                step(i)
            step(TILES - 1, last=True)
            for m in range(QB):
                for a in range(2):
                    sparse_hi_part(TILES - 1, m, a)

        @block.vector
        def _(dve):
            def f32(ap):
                return ap.bitcast(F32)

            def split_weight(n):
                raw, hi, lo, _, _ = SPLITS[n]
                dve.wait_ge(w_hi_ready, n + 1)
                nc.vector.tensor_tensor(lo[:, :], raw, f32(hi[:, :]), ALU.subtract).then_inc(w_ready, 1)

            def cond_lo(t):
                for h in range(KH):
                    dve.wait_ge(xc_hi_made, KH * t + h + 1)
                    nc.vector.tensor_tensor(xc_lo[:, h], front_ps[h][:], f32(xc_hi[:, h]),
                                            ALU.subtract).then_inc(front_freed, 1)

            def phi_sum(t, s):
                dve.wait_ge(phi_parts, 4 * t + s + 1)
                nc.vector.scalar_tensor_tensor(phi[:, s], expo[:, s % 2], 1.0, phi[:, s],
                                               ALU.min, ALU.add).then_inc(phi_made, 1)

            def kv_scan(t, d):
                dve.wait_ge(phi_made, 4 * t + 2 * d + 2)
                nc.vector.tensor_tensor_scan(kcs[:, d], carry[:], phi[:, 2 * d + 1], 0.0,
                                             ALU.mult, ALU.add).then_inc(attn_step[d], 1)
                dve.wait_ge(front_made, made(t, f"v{d}"))
                nc.vector.tensor_tensor(kvs[:, d], phi[:, 2 * d + 1], front_ps[d][:],
                                        ALU.mult).then_inc(front_freed, 1)
                dve.wait_ge(front_freed, freed(t, f"v{d}"))
                nc.vector.tensor_tensor_scan(kvs[:, d], carry[:], kvs[:, d], 0.0,
                                             ALU.mult, ALU.add).then_inc(attn_step[d], 1)

            def ratio_terms(t, d):
                dve.wait_ge(attn_step[d], STEPS * t + 1)
                nc.vector.tensor_tensor(kcs[:, d], phi[:, 2 * d], kcs[:, d], ALU.mult).then_inc(attn_step[d], 1)
                dve.wait_ge(attn_step[d], STEPS * t + 2)
                nc.vector.tensor_tensor(kvs[:, d], phi[:, 2 * d], kvs[:, d], ALU.mult).then_inc(attn_step[d], 1)

            def ratio(t, d):
                dve.wait_ge(guess_made, KH * t + d + 1)
                nc.vector.scalar_tensor_tensor(kcs[:, d], kcs[:, d], ATTN_EPS, guess[:, d],
                                               ALU.add, ALU.mult).then_inc(attn_step[d], 1)
                dve.wait_ge(attn_step[d], STEPS * t + 4)
                nc.vector.tensor_tensor(kvs[:, d], kvs[:, d], guess[:, d], ALU.mult).then_inc(attn_step[d], 1)
                dve.wait_ge(attn_step[d], STEPS * t + 6)
                nc.vector.scalar_tensor_tensor(kvs[:, d], kcs[:, d], 2.0, kvs[:, d],
                                               ALU.subtract, ALU.mult).then_inc(at_made, 1)

            def attn_lo(t, d):
                dve.wait_ge(at_hi_made, KH * t + d + 1)
                nc.vector.tensor_tensor(xc_lo[:, d], kvs[:, d], f32(xc_hi[:, d]), ALU.subtract).then_inc(at_ready, 1)

            def residual(t, h):
                dve.wait_ge(xcol_in, 16 * (t + 1))
                dve.wait_ge(front_made, made(t, f"out{h}"))
                if not (isinstance(t, int) and t == 0):
                    dve.wait_ge(held, t)
                nc.vector.scalar_tensor_tensor(x1[:, h], front_ps[BANK[f"out{h}"]][:], -HEAD_SCALE, xcol[:, h],
                                               ALU.mult, ALU.add).then_inc(front_freed, 1)

            def x1_lo_part(t, h):
                dve.wait_ge(x1_hi_made, KH * t + h + 1)
                nc.vector.tensor_tensor(x1_lo[:, h], x1[:, h], f32(x1_hi[:, h]), ALU.subtract).then_inc(x1_ready, 1)

            def mask_lora(t):
                dve.wait_ge(front_made, made(t, "xa"))
                own = lmask[:, bass.ds(t * BPT, BPT)].unsqueeze(2).to_broadcast([P, BPT, C])
                nc.vector.tensor_tensor(xa[:].rearrange("p (b l) -> p b l", l=C),
                                        front_ps[BANK["xa"]][:].rearrange("p (b l) -> p b l", l=C),
                                        own, ALU.mult).then_inc(front_freed, 1)

            def xa_lo_part(t):
                dve.wait_ge(xa_hi_made, t + 1)
                nc.vector.tensor_tensor(xa_lo[:], xa[:], f32(xa_hi[:]), ALU.subtract).then_inc(xa_ready, 1)

            def h2_lo_part(t, h):
                dve.wait_ge(h2_hi_made, KH * t + h + 1)
                nc.vector.tensor_tensor(h2_lo[:, h], front_ps[BANK[f"ada{h}"]][:], f32(h2_hi[:, h]),
                                        ALU.subtract).then_inc(front_freed, 1)

            def hidden(i, b, first=False):
                m, j = divmod(b, MEMB)
                if not first and j % 2 == 0:
                    dve.wait_ge(sparse_ready, NB * (i - 1) + MEMB * m + j + 2)
                dve.wait_ge(silu_made, NB * i + b + 1)
                dve.wait_ge(gu_made, 2 * (NB * i + b) + 2)
                nc.vector.tensor_tensor(hid[:, m, j], silu[:, b % 2], up_ps[b % 2][:], ALU.mult).then_inc(hid_made, 1)

            SEL = 9

            def select_compare(i, m):
                base = SEL * (QB * i + m)
                dve.wait_ge(mag_made, NB * i + MEMB * (m + 1))
                if not (isinstance(i, int) and i == 0 and m == 0):
                    dve.wait_ge(sparse_made, NB * i + MEMB * m)
                pairs = mag[:, m].rearrange("p (a b) n -> p a b n", b=2)
                nc.vector.tensor_tensor(inner[:], pairs[:, :, 0], pairs[:, :, 1], ALU.is_ge).then_inc(sel_step, 1)
                nc.vector.tensor_tensor(beats[:, 0], mag[:, m, 0:2], mag[:, m, 2:4], ALU.is_ge).then_inc(sel_step, 1)
                nc.vector.tensor_tensor(beats[:, 1, 0], mag[:, m, 0], mag[:, m, 3], ALU.is_ge).then_inc(sel_step, 1)
                nc.vector.tensor_tensor(beats[:, 1, 1], mag[:, m, 1], mag[:, m, 2], ALU.is_ge).then_inc(sel_step, 1)
                return base

            def select_count(i, m):
                base = SEL * (QB * i + m)
                dve.wait_ge(sel_step, base + 1)
                nc.vector.tensor_scalar(inner[:], inner[:], 3.0, None, ALU.mult).then_inc(sel_step, 1)
                dve.wait_ge(sel_step, base + 4)
                nc.vector.tensor_tensor(beats[:, 0], beats[:, 0], beats[:, 1], ALU.add).then_inc(sel_step, 1)
                dve.wait_ge(sel_step, base + 6)
                nc.vector.tensor_tensor(wins[:], beats[:, 0, 0], beats[:, 0, 1], ALU.add).then_inc(sel_step, 1)

            def select_rank(i, m):
                base = SEL * (QB * i + m)
                both = wins[:].unsqueeze(1).to_broadcast([P, 2, NT])
                dve.wait_ge(sel_step, base + 7)
                nc.vector.tensor_tensor(beats[:, 0], both, inner[:], ALU.add).then_inc(sel_step, 1)
                nc.vector.tensor_tensor(beats[:, 1], both, inner[:], ALU.subtract).then_inc(sel_step, 1)

            def select_keep(i, m):
                base = SEL * (QB * i + m)
                dve.wait_ge(sel_step, base + 9)
                for j, (rank, bound, op) in enumerate([
                        (beats[:, 0, 0], 4.0, ALU.is_ge), (beats[:, 1, 0], 1.0, ALU.is_ge),
                        (beats[:, 1, 1], 0.0, ALU.is_le), (beats[:, 0, 1], 3.0, ALU.is_le)]):
                    nc.vector.scalar_tensor_tensor(hid[:, m, j], rank, bound, hid[:, m, j],
                                                   op, ALU.mult).then_inc(sparse_made, 1)

            def sparse_lo_part(i, m, a):
                dve.wait_ge(sparse_hi_made, 2 * (QB * i + m) + a + 1)
                nc.vector.tensor_tensor(sparse_lo[:, 2 * a:2 * (a + 1)], hid[:, m, 2 * a:2 * (a + 1)],
                                        f32(sparse_hi[:, 2 * a:2 * (a + 1)]), ALU.subtract).then_inc(sparse_ready, 2)

            def result(i, last=False):
                for h in range(KH):
                    dve.wait_ge(down_made, NB * (i + 1))
                    dve.wait_ge(held, i + 1)
                    if last and not h:
                        dve.wait_ge(y_stored, 16 * i)
                    nc.vector.tensor_tensor(y[:, h], down_ps[h][:], x1_held[:, h], ALU.add).then_inc(y_made, 1)

            def step(i, first=False, last=False):
                t = i + 1
                if not last:
                    cond_lo(t)
                if not first:
                    select_compare(i - 1, 1)
                    sparse_lo_part(i - 1, 0, 0)
                if not last:
                    phi_sum(t, 0)
                if not first:
                    select_count(i - 1, 1)
                    sparse_lo_part(i - 1, 0, 1)
                    select_rank(i - 1, 1)
                if not last:
                    phi_sum(t, 1)
                if not first:
                    select_keep(i - 1, 1)
                    sparse_lo_part(i - 1, 1, 0)
                hidden(i, 0, first)
                if not last:
                    phi_sum(t, 2)
                    kv_scan(t, 0)
                    phi_sum(t, 3)
                if not first:
                    sparse_lo_part(i - 1, 1, 1)
                if not last:
                    ratio_terms(t, 0)
                    kv_scan(t, 1)
                    ratio_terms(t, 1)
                hidden(i, 1, first)
                if not first:
                    result(i - 1)
                if not last:
                    ratio(t, 0)
                hidden(i, 2, first)
                if not last:
                    ratio(t, 1)
                hidden(i, 3, first)
                if not last:
                    attn_lo(t, 0)
                    attn_lo(t, 1)
                select_compare(i, 0)
                hidden(i, 4, first)
                if not last:
                    residual(t, 0)
                    residual(t, 1)
                    x1_lo_part(t, 0)
                    x1_lo_part(t, 1)
                hidden(i, 5, first)
                select_count(i, 0)
                if not last:
                    mask_lora(t)
                select_rank(i, 0)
                hidden(i, 6, first)
                if not last:
                    xa_lo_part(t)
                hidden(i, 7, first)
                select_keep(i, 0)
                if not last:
                    h2_lo_part(t, 0)
                    h2_lo_part(t, 1)

            dve.wait_ge(tables_in, 48)
            nc.vector.tensor_scalar(lmask[:], aidx[:], lid[:], lscale[:], ALU.is_equal,
                                    ALU.mult).then_inc(mask_ready, 1)
            for n in range(PROJ_SPLIT):
                split_weight(n)
            cond_lo(0)
            for s in range(4):
                phi_sum(0, s)
            dve.wait_ge(tables_ready, 3)
            kv_scan(0, 0)
            kv_scan(0, 1)
            ratio_terms(0, 0)
            ratio_terms(0, 1)
            ratio(0, 0)
            attn_lo(0, 0)
            ratio(0, 1)
            attn_lo(0, 1)
            for n in range(PROJ_SPLIT, ALL_SPLIT):
                split_weight(n)
            residual(0, 0)
            residual(0, 1)
            x1_lo_part(0, 0)
            x1_lo_part(0, 1)
            dve.wait_ge(mask_ready, 1)
            mask_lora(0)
            xa_lo_part(0)
            h2_lo_part(0, 0)
            h2_lo_part(0, 1)
            step(0, first=True)
            with dve.Fori(1, TILES - 1) as i:
                step(i)
            step(TILES - 1, last=True)
            for a in range(2):
                sparse_lo_part(TILES - 1, 0, a)
            select_compare(TILES - 1, 1)
            select_count(TILES - 1, 1)
            select_rank(TILES - 1, 1)
            select_keep(TILES - 1, 1)
            for a in range(2):
                sparse_lo_part(TILES - 1, 1, a)
            result(TILES - 1, last=True)


def kernel(**inputs):
    import numpy as _np
    import concourse.bacc as _bacc
    from concourse.bass_utils import run_bass_kernel_spmd as _run

    g = {k: _np.asarray(v) for k, v in inputs.items()}
    x = g["x"]
    B, C, T = x.shape
    rows = x.reshape(B * C, T)
    NA, RANK, _ = g["L0_cond2_A"].shape
    S = g["L0_cond_weights"].shape[0]
    GATE = g["L0_ffn_w_gate"].shape

    def members(w):
        return w.reshape(GATE[0], GATE[1] // 4, 4).transpose(0, 2, 1)

    arrays = {
        "x_rows": rows,
        "x_cols": rows.T,
        "cond_idx": g["itok_B_1_198"].reshape(B, 1),
        "adapter_idx": g["itok_B_0_6"].reshape(1, B),
        "cond_w": g["L0_cond_weights"].reshape(S, C * C),
        "w_qkv": g["L0_attn_W_qkv"].T,
        "w_out": g["L0_attn_W_out"].T,
        "w_ada": g["L0_cond2_W"].T,
        "lora_a": g["L0_cond2_A"].reshape(NA * RANK, T).T,
        "lora_b": g["L0_cond2_Bm"].transpose(0, 2, 1).reshape(NA * RANK, T),
        "lora_scale": _np.repeat(g["L0_cond2_scalings"], RANK).reshape(NA * RANK, 1),
        "lora_id": _np.repeat(_np.arange(NA, dtype=_np.float32), RANK).reshape(NA * RANK, 1),
        "w_gate": members(g["L0_ffn_w_gate"]),
        "w_up": members(g["L0_ffn_w_up"]),
        "w_down": g["L0_ffn_w_down"].reshape(GATE[1] // 4, 4 * T),
    }
    nc = _bacc.Bacc("TRN2", target_bir_lowering=False, num_devices=1)
    arrays = {f"in_{k}": _np.ascontiguousarray(v) for k, v in arrays.items()}
    args = [nc.dram_tensor(k, v.shape, mybir.dt.from_np(v.dtype), kind="ExternalInput").ap()
            for k, v in arrays.items()]
    args.append(nc.dram_tensor("out_y", (T, B * C), F32, kind="ExternalOutput").ap())
    adaln_attn_ffn(nc, *args)
    r = _run(nc, [arrays], core_ids=[0])
    return r.results[0]["out_y"].T.reshape(B, C, T)
```

```python
from contextlib import ExitStack

import concourse.bass as bass
from concourse import mybir

F32 = mybir.dt.float32
F32R = mybir.dt.float32r
BF16 = mybir.dt.bfloat16
I32 = mybir.dt.int32
U32 = mybir.dt.uint32
ALU = mybir.AluOpType
ACT = mybir.ActivationFunctionType

P = 128
ATTN_EPS = 1e-09


def adaln_attn_ffn(
    nc: bass.Bass,
    x_rows: bass.AP,
    x_cols: bass.AP,
    cond_idx: bass.AP,
    adapter_idx: bass.AP,
    cond_w: bass.AP,
    w_qkv: bass.AP,
    w_out: bass.AP,
    w_ada: bass.AP,
    lora_a: bass.AP,
    lora_b: bass.AP,
    lora_scale: bass.AP,
    lora_id: bass.AP,
    w_gate: bass.AP,
    w_up: bass.AP,
    w_down: bass.AP,
    y_cols: bass.AP,
):
    ROWS, T = x_rows.shape
    B = cond_idx.shape[0]
    C = ROWS // B
    NT = 512
    TILES = ROWS // NT
    KH = T // P
    GRP = NT // P
    BPG = P // C
    BPT = NT // C
    MEMB = w_gate.shape[1]
    QB = w_gate.shape[2] // P
    NB = QB * MEMB
    HEAD_SCALE = 16 ** -0.5
    STEPS = 6
    assert KH == 2 and MEMB == 4 and QB == 2 and lora_b.shape[0] == P and B == P

    FRONT = ["cond0", "cond1", "k0", "q0", "k1", "q1", "v0", "v1", "out0", "out1", "xa", "ada0", "ada1"]
    FRONT_FIRST = ["cond0", "cond1", "k0", "v0", "q0", "k1", "v1", "q1", "out0", "out1", "xa", "ada0", "ada1"]
    BANK = {"cond0": 1, "cond1": 0, "k0": 0, "q0": 1, "k1": 0, "q1": 1, "v0": 0, "v1": 1,
            "out0": 0, "out1": 1, "xa": 0, "ada0": 1, "ada1": 0}
    BANK_FIRST = {"cond0": 1, "cond1": 0, "k0": 2, "v0": 3, "q0": 4, "k1": 5, "v1": 6, "q1": 7,
                  "out0": 0, "out1": 1, "xa": 2, "ada0": 1, "ada1": 0}
    FREED = ["cond0", "cond1", "v0", "v1", "out0", "out1", "xa", "ada0", "ada1"]
    NF, NV = len(FRONT), len(FREED)

    def is_first(t):
        return isinstance(t, int) and t == 0

    def made(t, name):
        return NF * t + (FRONT_FIRST if is_first(t) else FRONT).index(name) + 1

    def freed(t, name):
        return NV * t + FREED.index(name) + 1

    ctx = ExitStack()
    with ctx:
        def sb(name, shape, dt=F32):
            return ctx.enter_context(nc.sbuf_tensor(name, shape, dt))

        def bank(name):
            return ctx.enter_context(nc.psum_tensor(name, [P, NT], F32))

        def sem(name):
            return ctx.enter_context(nc.semaphore(name))

        qkv_hi, qkv_lo = (sb(f"qkv_{s}", [P, KH, 3 * T], F32R) for s in ("hi", "lo"))
        wo_hi, wo_lo = (sb(f"wo_{s}", [P, KH, T], F32R) for s in ("hi", "lo"))
        wa_hi, wa_lo = (sb(f"wa_{s}", [P, KH, T], F32R) for s in ("hi", "lo"))
        la_hi, la_lo = (sb(f"la_{s}", [P, KH, P], F32R) for s in ("hi", "lo"))
        lb_hi, lb_lo = (sb(f"lb_{s}", [P, T], F32R) for s in ("hi", "lo"))
        gate_hi, gate_lo = (sb(f"gate_{s}", [P, KH, MEMB, QB * P], F32R) for s in ("hi", "lo"))
        up_hi, up_lo = (sb(f"up_{s}", [P, KH, MEMB, QB * P], F32R) for s in ("hi", "lo"))
        wd_hi, wd_lo = (sb(f"wd_{s}", [P, QB, MEMB, T], F32R) for s in ("hi", "lo"))
        hid = sb("hid", [P, QB, MEMB, NT])
        mag = sb("mag", [P, QB, MEMB, NT])
        sparse_hi, sparse_lo = (sb(f"sparse_{s}", [P, MEMB, NT], F32R) for s in ("hi", "lo"))
        raw_gate = hid[:, 0].rearrange("p j n -> p (j n)").rearrange("p (h j q) -> p h j q", h=KH, j=MEMB)
        raw_up = hid[:, 1].rearrange("p j n -> p (j n)").rearrange("p (h j q) -> p h j q", h=KH, j=MEMB)
        raw_s = mag[:, :].rearrange("p m j n -> p (m j n)")
        at = 0
        raws = []
        for n in (KH * 3 * T, KH * T, KH * T, KH * P, T):
            raws.append(raw_s[:, at:at + n])
            at += n
        raw_qkv, raw_wo, raw_wa, raw_la = (r.rearrange("p (h n) -> p h n", h=KH) for r in raws[:4])
        raw_lb = raws[4]
        y = sb("y", [P, KH, NT])
        raw_wd = [r.rearrange("p (j n) -> p j n", j=MEMB)
                  for r in (raw_s[:, at:at + MEMB * T], y[:].rearrange("p h n -> p (h n)"))]

        xrow = sb("xrow", [P, GRP, T])
        bdiag = sb("bdiag", [P, GRP, P])
        xcol = sb("xcol", [P, KH, NT])
        xc_hi, xc_lo = (sb(f"xc_{s}", [P, KH, NT], F32R) for s in ("hi", "lo"))
        expo = sb("expo", [P, 2, NT])
        phi = sb("phi", [P, 4, NT])
        kvs = sb("kvs", [P, KH, NT])
        kcs = sb("kcs", [P, KH, NT])
        guess = expo
        eps = sb("eps", [P, 1])
        x1 = sb("x1", [P, KH, NT])
        x1_hi, x1_lo = (sb(f"x1_{s}", [P, KH, NT], F32R) for s in ("hi", "lo"))
        xa = sb("xa", [P, NT])
        xa_hi, xa_lo = (sb(f"xa_{s}", [P, NT], F32R) for s in ("hi", "lo"))
        h2_hi, h2_lo = (sb(f"h2_{s}", [P, KH, NT], F32R) for s in ("hi", "lo"))
        silu = sb("silu", [P, 2, NT])
        beats = sb("beats", [P, 2, 2, NT], BF16)
        inner = sb("inner", [P, 2, NT], BF16)
        wins = sb("wins", [P, NT], BF16)
        x1_held = sb("x1_held", [P, KH, NT])
        carry = sb("carry", [P, NT])
        cidx = sb("cidx", [P, 1], I32)
        aidx = sb("aidx", [P, B], I32)
        lscale = sb("lscale", [P, 1])
        lid = sb("lid", [P, 1])
        lmask = sb("lmask", [P, B])
        gathered = hid[:, 0].rearrange("p j n -> p (j n)")[:, 0:C * C]
        gathered_first = hid[:, 1].rearrange("p j n -> p (j n)")[:, 0:C * C]
        w_sel = nc.dram_tensor("w_sel", (B, C * C), F32).ap()

        gate_ps = [bank(f"gate_ps{n}") for n in range(2)]
        up_ps = [bank(f"up_ps{n}") for n in range(2)]
        down_ps = [bank(f"down_ps{n}") for n in range(KH)]
        front_ps = [bank(f"front_ps{n}") for n in range(2)]
        all_ps = front_ps + gate_ps + up_ps + down_ps

        def front_bank(t, name):
            return all_ps[(BANK_FIRST if is_first(t) else BANK)[name]][:]


        idx_in = sem("idx_in")
        gather_first_in = sem("gather_first_in")
        gather_in = sem("gather_in")
        gather_out = sem("gather_out")
        bdiag_zero = sem("bdiag_zero")
        tables_in = sem("tables_in")
        qkv_in, wproj_in, gate_in, up_in, wd_in = (sem(f"{n}_in") for n in ("qkv", "wproj", "gate", "up", "wd"))
        w_hi_ready = sem("w_hi_ready")
        w_ready = sem("w_ready")
        tables_ready = sem("tables_ready")
        mask_ready = sem("mask_ready")
        xrow_in, bdiag_in, xcol_in = sem("xrow_in"), sem("bdiag_in"), sem("xcol_in")
        front_made = sem("front_made")
        front_freed = sem("front_freed")
        phi_parts = sem("phi_parts")
        phi_made = sem("phi_made")
        xc_hi_made, at_hi_made, x1_hi_made, xa_hi_made, h2_hi_made = (
            sem(f"{n}_hi_made") for n in ("xc", "at", "x1", "xa", "h2"))
        attn_step = [sem(f"attn_step{d}") for d in range(KH)]
        ln_made, guess_made, at_made = sem("ln_made"), sem("guess_made"), sem("at_made")
        at_ready, x1_ready, xa_ready = sem("at_ready"), sem("x1_ready"), sem("xa_ready")
        gu_made = sem("gu_made")
        silu_made = sem("silu_made")
        hid_made = sem("hid_made")
        mag_made = sem("mag_made")
        sel_step = sem("sel_step")
        sparse_made = sem("sparse_made")
        sparse_hi_made = sem("sparse_hi_made")
        sparse_ready = sem("sparse_ready")
        down_made = sem("down_made")
        y_made = sem("y_made")
        y_stored = sem("y_stored")
        held = sem("held")

        SPLITS = [
            (raw_qkv[:, 0], qkv_hi[:, 0], qkv_lo[:, 0], qkv_in, 16),
            (raw_qkv[:, 1], qkv_hi[:, 1], qkv_lo[:, 1], qkv_in, 16),
            (raw_wo, wo_hi, wo_lo, wproj_in, 64),
            (raw_wa, wa_hi, wa_lo, wproj_in, 64),
            (raw_la, la_hi, la_lo, wproj_in, 64),
            (raw_lb, lb_hi, lb_lo, wproj_in, 64),
            (raw_gate[:, 0], gate_hi[:, 0], gate_lo[:, 0], gate_in, 16),
            (raw_gate[:, 1], gate_hi[:, 1], gate_lo[:, 1], gate_in, 16),
            (raw_up[:, 0], up_hi[:, 0], up_lo[:, 0], up_in, 16),
            (raw_up[:, 1], up_hi[:, 1], up_lo[:, 1], up_in, 16),
            (raw_wd[0], wd_hi[:, 0], wd_lo[:, 0], wd_in, 32),
            (raw_wd[1], wd_hi[:, 1], wd_lo[:, 1], wd_in, 32),
        ]
        QKV_SPLIT, OUT_SPLIT, PROJ_SPLIT, GATE_UP_SPLIT, ALL_SPLIT = 2, 3, 6, 10, len(SPLITS)

        block = ctx.enter_context(nc.Block())

        @block.sync
        def _(sp):
            xrow_v = x_rows.rearrange("(n g p) t -> n p g t", g=GRP, p=P)
            xcol_v = x_cols.rearrange("(h p) (n r) -> n p h r", p=P, r=NT)
            wsel_v = w_sel.rearrange("(n g j) (c d) -> n j c g d", g=GRP, j=BPG, c=C)
            y_v = y_cols.rearrange("(h p) (n r) -> n p h r", p=P, r=NT)

            def load_front(t):
                if not is_first(t):
                    sp.wait_ge(front_made, made(t - 1, "cond1"))
                sp.dma_start(xrow[:], xrow_v[t]).then_inc(xrow_in, 16)
                for j in range(BPG):
                    sp.dma_start(bdiag[C * j:C * (j + 1), :, C * j:C * (j + 1)], wsel_v[t, j]).then_inc(bdiag_in, 16)

            def load_xcol(t, stored=None):
                if not is_first(t):
                    taken = freed(t - 1, "out1")
                    if stored is not None:
                        taken, stored = sp.snap(taken), sp.snap(16 * stored)
                        sp.wait_ge(y_stored, stored)
                    sp.wait_ge(front_freed, taken)
                sp.dma_start(xcol[:], xcol_v[t]).then_inc(xcol_in, 16)

            def store(i):
                sp.wait_ge(y_made, KH * (i + 1))
                sp.dma_start(y_v[i], y[:]).then_inc(y_stored, 16)

            sp.dma_start(cidx[:], cond_idx).then_inc(idx_in, 16)
            sp.dma_start(xrow[:], xrow_v[0]).then_inc(xrow_in, 16)
            sp.wait_ge(gather_first_in, 16)
            sp.dma_start(w_sel[0:BPT], gathered_first[0:BPT]).then_inc(gather_out, 16)
            sp.wait_ge(gather_out, 16)
            sp.wait_ge(bdiag_zero, 1)
            for j in range(BPG):
                sp.dma_start(bdiag[C * j:C * (j + 1), :, C * j:C * (j + 1)], wsel_v[0, j]).then_inc(bdiag_in, 16)
            sp.wait_ge(gather_in, 16)
            sp.dma_start(w_sel[BPT:B], gathered[BPT:B]).then_inc(gather_out, 16)
            load_xcol(0)
            sp.wait_ge(gather_out, 32)
            sp.dma_start(raw_gate, w_gate.rearrange("(h p) j q -> p h j q", p=P)).then_inc(gate_in, 16)
            sp.dma_start(raw_up, w_up.rearrange("(h p) j q -> p h j q", p=P)).then_inc(up_in, 16)
            for m in range(QB):
                sp.dma_start(raw_wd[m], w_down[P * m:P * (m + 1)].rearrange("p (j n) -> p j n", j=MEMB)).then_inc(wd_in, 16)
            load_front(1)
            load_xcol(1)
            with sp.Fori(1, TILES - 1) as i:
                load_front(i + 1)
                store(i - 1)
                load_xcol(i + 1, stored=i)
            store(TILES - 2)
            store(TILES - 1)
            sp.wait_ge(y_stored, 16 * TILES)

        @block.gpsimd
        def _(pool):
            nc.gpsimd.memset(bdiag[:], 0.0).then_inc(bdiag_zero, 1)
            pool.wait_ge(idx_in, 16)
            for out, n, arrived in ((gathered_first, BPT, gather_first_in), (gathered, B, gather_in)):
                nc.gpsimd.indirect_dma_start(
                    out=out[0:n], out_offset=None, in_=cond_w,
                    in_offset=bass.IndirectOffsetOnAxis(ap=cidx[0:n, 0:1].bitcast(U32), axis=0)).then_inc(arrived, 16)
            nc.gpsimd.memset(eps[:], ATTN_EPS).then_inc(tables_ready, 1)
            nc.gpsimd.memset(carry[:], 1.0).then_inc(tables_ready, 1)
            pool.wait_ge(tables_ready, 2)
            nc.gpsimd.memset(carry[:].rearrange("p (b l) -> p b l", l=C)[:, :, 0:1], 0.0).then_inc(tables_ready, 1)

        @block.tensor
        def _(pe):
            def split_product(ps, terms, start=True, stop=True):
                for n, (w_hi, w_lo, v_hi, v_lo) in enumerate(terms):
                    nc.tensor.matmul(ps, w_hi, v_lo, start=start and n == 0, stop=False)
                    nc.tensor.matmul(ps, w_lo, v_hi, start=False, stop=False)
                    last = nc.tensor.matmul(ps, w_hi, v_hi, start=False, stop=stop and n == len(terms) - 1)
                return last

            def cond(t):
                pe.wait_ge(xrow_in, 16 * (t + 1))
                pe.wait_ge(bdiag_in, 16 * BPG * (t + 1))
                for h in range(KH):
                    if not is_first(t):
                        pe.wait_ge(front_freed, freed(t - 1, f"ada{h}"))
                    for g in range(GRP):
                        last = nc.tensor.matmul(front_bank(t, f"cond{h}")[:, P * g:P * (g + 1)],
                                                xrow[:, g, P * h:P * (h + 1)], bdiag[:, g, :], start=True, stop=True)
                    last.then_inc(front_made, 1)

            BANK_READ = {"k0": (front_freed, freed(0, "cond1"), NV), "q0": (front_freed, freed(0, "cond0"), NV),
                         "k1": (phi_parts, 1, 4), "q1": (phi_parts, 2, 4),
                         "v0": (phi_parts, 3, 4), "v1": (phi_parts, 4, 4)}

            def project(t, name):
                col = T * "qkv".index(name[0]) + P * int(name[1])
                if is_first(t):
                    if name == "k0":
                        pe.wait_ge(w_ready, QKV_SPLIT)
                        pe.wait_ge(front_freed, freed(t, "cond1"))
                else:
                    read, count, per_tile = BANK_READ[name]
                    pe.wait_ge(read, per_tile * t + count)
                split_product(front_bank(t, name), [
                    (qkv_hi[:, k, col:col + P], qkv_lo[:, k, col:col + P], xc_hi[:, k], xc_lo[:, k])
                    for k in range(KH)]).then_inc(front_made, 1)

            def out_proj(t):
                if is_first(t):
                    pe.wait_ge(w_ready, OUT_SPLIT)
                pe.wait_ge(at_ready, KH * (t + 1))
                for h in range(KH):
                    split_product(front_bank(t, f"out{h}"), [
                        (wo_hi[:, k, P * h:P * (h + 1)], wo_lo[:, k, P * h:P * (h + 1)], xc_hi[:, k], xc_lo[:, k])
                        for k in range(KH)]).then_inc(front_made, 1)

            def lora_in(t):
                if is_first(t):
                    pe.wait_ge(w_ready, PROJ_SPLIT)
                pe.wait_ge(x1_ready, KH * (t + 1))
                split_product(front_bank(t, "xa"), [
                    (la_hi[:, k], la_lo[:, k], x1_hi[:, k], x1_lo[:, k]) for k in range(KH)]).then_inc(front_made, 1)

            def adapted(t):
                def from_x1(h):
                    cols = slice(P * h, P * (h + 1))
                    split_product(front_bank(t, f"ada{h}"), [
                        (wa_hi[:, k, cols], wa_lo[:, k, cols], x1_hi[:, k], x1_lo[:, k]) for k in range(KH)], stop=False)

                def from_adapter(h):
                    cols = slice(P * h, P * (h + 1))
                    split_product(front_bank(t, f"ada{h}"), [(lb_hi[:, cols], lb_lo[:, cols], xa_hi[:], xa_lo[:])],
                                  start=False).then_inc(front_made, 1)

                from_x1(0)
                if is_first(t):
                    from_x1(1)
                pe.wait_ge(xa_ready, t + 1)
                from_adapter(0)
                if not is_first(t):
                    from_x1(1)
                from_adapter(1)

            def gate_up(i, b, first=False):
                m, j = divmod(b, MEMB)
                cols = slice(P * m, P * (m + 1))
                if b == 0:
                    pe.wait_ge(front_freed, freed(i, "ada1"))
                    if first:
                        pe.wait_ge(w_ready, GATE_UP_SPLIT)
                if not (first and b < 2):
                    pe.wait_ge(silu_made, NB * i + b - 1)
                split_product(gate_ps[b % 2][:], [
                    (gate_hi[:, k, j, cols], gate_lo[:, k, j, cols], h2_hi[:, k], h2_lo[:, k])
                    for k in range(KH)]).then_inc(gu_made, 1)
                if not (first and b < 2):
                    pe.wait_ge(hid_made, NB * i + b - 1)
                split_product(up_ps[b % 2][:], [
                    (up_hi[:, k, j, cols], up_lo[:, k, j, cols], h2_hi[:, k], h2_lo[:, k])
                    for k in range(KH)]).then_inc(gu_made, 1)

            def down(i, m):
                if is_first(i) and m == 0:
                    pe.wait_ge(w_ready, ALL_SPLIT)
                if m == 0:
                    pe.wait_ge(held, i + 1)
                for j in range(MEMB):
                    pe.wait_ge(sparse_ready, NB * i + MEMB * m + j + 1)
                    for h in range(KH):
                        cols = slice(P * h, P * (h + 1))
                        last = split_product(
                            down_ps[h][:], [(wd_hi[:, m, j, cols], wd_lo[:, m, j, cols], sparse_hi[:, j], sparse_lo[:, j])],
                            start=(m == 0 and j == 0), stop=(m == QB - 1 and j == MEMB - 1))
                    last.then_inc(down_made, 1)

            def step(i, first=False, last=False):
                if not last:
                    cond(i + 1)
                gate_up(i, 0, first)
                if not last:
                    project(i + 1, "k0")
                    project(i + 1, "q0")
                    project(i + 1, "k1")
                    project(i + 1, "q1")
                    project(i + 1, "v0")
                gate_up(i, 1, first)
                if not last:
                    project(i + 1, "v1")
                if not first:
                    down(i - 1, 1)
                gate_up(i, 2, first)
                gate_up(i, 3, first)
                gate_up(i, 4, first)
                gate_up(i, 5, first)
                if not last:
                    out_proj(i + 1)
                gate_up(i, 6, first)
                if not last:
                    lora_in(i + 1)
                gate_up(i, 7, first)
                if not last:
                    adapted(i + 1)
                down(i, 0)

            cond(0)
            project(0, "k0")
            project(0, "v0")
            project(0, "q0")
            project(0, "k1")
            project(0, "v1")
            project(0, "q1")
            out_proj(0)
            lora_in(0)
            adapted(0)
            step(0, first=True)
            with pe.Fori(1, TILES - 1) as i:
                step(i)
            step(TILES - 1, last=True)
            down(TILES - 1, 1)

        @block.scalar
        def _(act):
            def exp_ln_set():
                nc.scalar.preload_act_table_set("natural_log_exp_and_others")

            def silu_set():
                nc.scalar.preload_act_table_set("silu_and_others")

            def split_weight(n):
                raw, hi, _, arrived, count = SPLITS[n]
                act.wait_ge(arrived, count)
                nc.scalar.copy(hi[:] if len(hi.shape) < 3 else hi[:, :], raw).then_inc(w_hi_ready, 1)

            def cond_hi(t):
                for h in range(KH):
                    act.wait_ge(front_made, made(t, f"cond{h}"))
                    nc.scalar.copy(xc_hi[:, h], front_bank(t, f"cond{h}")).then_inc(xc_hi_made, 1)

            PHI = ["k0", "q0", "k1", "q1"]

            def phi_terms(t, s):
                ps = front_bank(t, PHI[s])
                act.wait_ge(front_made, made(t, PHI[s]))
                if s >= 2:
                    act.wait_ge(phi_made, 4 * t + s - 1)
                elif not is_first(t):
                    act.wait_ge(phi_made, 4 * t + s - 1)
                if s == 0 and not is_first(t):
                    act.wait_ge(at_ready, KH * t)
                nc.scalar.activation(expo[:, s % 2], ps, ACT.Exp)
                nc.scalar.activation(phi[:, s], ps, ACT.Relu).then_inc(phi_parts, 1)

            def guess_inverse(t, d):
                act.wait_ge(attn_step[d], STEPS * t + 3)
                if d == 0:
                    act.wait_ge(phi_made, 4 * (t + 1))
                nc.scalar.activation(guess[:, d], kcs[:, d], ACT.Ln, bias=eps[:]).then_inc(ln_made, 1)
                act.wait_ge(ln_made, KH * t + d + 1)
                nc.scalar.activation(guess[:, d], guess[:, d], ACT.Exp, scale=-1.0).then_inc(guess_made, 1)

            def attn_hi(t, d):
                act.wait_ge(at_made, KH * t + d + 1)
                act.wait_ge(front_made, made(t, "q1" if is_first(t) else "v1"))
                nc.scalar.copy(xc_hi[:, d], kvs[:, d]).then_inc(at_hi_made, 1)

            def x1_hi_part(t, h):
                act.wait_ge(front_freed, freed(t, f"out{h}"))
                nc.scalar.copy(x1_hi[:, h], x1[:, h]).then_inc(x1_hi_made, 1)

            def xa_hi_part(t):
                act.wait_ge(front_freed, freed(t, "xa"))
                nc.scalar.copy(xa_hi[:], xa[:]).then_inc(xa_hi_made, 1)

            def h2_hi_part(t, h):
                act.wait_ge(front_made, made(t, f"ada{h}"))
                nc.scalar.copy(h2_hi[:, h], front_bank(t, f"ada{h}")).then_inc(h2_hi_made, 1)

            def silu_gate(i, b, first=False):
                act.wait_ge(gu_made, 2 * (NB * i + b) + 1)
                if not (first and b < 2):
                    act.wait_ge(hid_made, NB * i + b - 1)
                nc.scalar.activation(silu[:, b % 2], gate_ps[b % 2][:], ACT.Silu).then_inc(silu_made, 1)

            def magnitude(i, b):
                m, j = divmod(b, MEMB)
                act.wait_ge(hid_made, NB * i + b + 1)
                nc.scalar.activation(mag[:, m, j], hid[:, m, j], ACT.Abs).then_inc(mag_made, 1)

            def sparse_hi_part(i, m, a):
                act.wait_ge(sparse_made, NB * i + MEMB * m + 2 * (a + 1))
                if not (is_first(i) and m == 0):
                    act.wait_ge(down_made, NB * i + MEMB * (m - 1) + 2 * (a + 1))
                nc.scalar.copy(sparse_hi[:, 2 * a:2 * (a + 1)], hid[:, m, 2 * a:2 * (a + 1)]).then_inc(sparse_hi_made, 1)

            def hold_x1(i):
                if not is_first(i):
                    act.wait_ge(y_made, KH * i)
                nc.scalar.copy(x1_held[:], x1[:]).then_inc(held, 1)

            def step(i, first=False, last=False):
                t = i + 1
                if not last:
                    cond_hi(t)
                silu_gate(i, 0, first)
                if not last:
                    exp_ln_set()
                    phi_terms(t, 0)
                    phi_terms(t, 1)
                    phi_terms(t, 2)
                if not first:
                    sparse_hi_part(i - 1, 1, 0)
                if not last:
                    phi_terms(t, 3)
                    silu_set()
                silu_gate(i, 1, first)
                magnitude(i, 0)
                if not first:
                    sparse_hi_part(i - 1, 1, 1)
                if not last:
                    exp_ln_set()
                    guess_inverse(t, 0)
                    guess_inverse(t, 1)
                    silu_set()
                silu_gate(i, 2, first)
                if not last:
                    attn_hi(t, 0)
                magnitude(i, 1)
                silu_gate(i, 3, first)
                magnitude(i, 2)
                if not last:
                    attn_hi(t, 1)
                magnitude(i, 3)
                silu_gate(i, 4, first)
                silu_gate(i, 5, first)
                hold_x1(i)
                if not last:
                    x1_hi_part(t, 0)
                    x1_hi_part(t, 1)
                silu_gate(i, 6, first)
                magnitude(i, 4)
                magnitude(i, 5)
                magnitude(i, 6)
                if not last:
                    xa_hi_part(t)
                sparse_hi_part(i, 0, 0)
                if not last:
                    h2_hi_part(t, 0)
                silu_gate(i, 7, first)
                sparse_hi_part(i, 0, 1)
                if not last:
                    h2_hi_part(t, 1)
                magnitude(i, 7)

            act.dma_start(aidx[:], adapter_idx.to_broadcast([P, B])).then_inc(tables_in, 16)
            act.dma_start(lscale[:], lora_scale).then_inc(tables_in, 16)
            act.dma_start(lid[:], lora_id).then_inc(tables_in, 16)
            act.dma_start(raw_qkv, w_qkv.rearrange("(h p) n -> p h n", p=P)).then_inc(qkv_in, 16)
            act.dma_start(raw_wo, w_out.rearrange("(h p) n -> p h n", p=P)).then_inc(wproj_in, 16)
            act.dma_start(raw_wa, w_ada.rearrange("(h p) n -> p h n", p=P)).then_inc(wproj_in, 16)
            act.dma_start(raw_la, lora_a.rearrange("(h p) n -> p h n", p=P)).then_inc(wproj_in, 16)
            act.dma_start(raw_lb, lora_b).then_inc(wproj_in, 16)
            exp_ln_set()
            split_weight(0)
            split_weight(1)
            split_weight(2)
            split_weight(3)
            cond_hi(0)
            split_weight(4)
            phi_terms(0, 0)
            phi_terms(0, 1)
            phi_terms(0, 2)
            split_weight(5)
            split_weight(6)
            phi_terms(0, 3)
            act.wait_ge(tables_ready, 3)
            guess_inverse(0, 0)
            guess_inverse(0, 1)
            silu_set()
            attn_hi(0, 0)
            split_weight(7)
            attn_hi(0, 1)
            x1_hi_part(0, 0)
            x1_hi_part(0, 1)
            split_weight(8)
            split_weight(9)
            xa_hi_part(0)
            split_weight(10)
            split_weight(11)
            h2_hi_part(0, 0)
            h2_hi_part(0, 1)
            step(0, first=True)
            with act.Fori(1, TILES - 1) as i:
                step(i)
            step(TILES - 1, last=True)
            for a in range(2):
                sparse_hi_part(TILES - 1, 1, a)

        @block.vector
        def _(dve):
            def f32(ap):
                return ap.bitcast(F32)

            def split_weight(n):
                raw, hi, lo, _, _ = SPLITS[n]
                dve.wait_ge(w_hi_ready, n + 1)
                nc.vector.tensor_tensor(lo[:, :], raw, f32(hi[:, :]), ALU.subtract).then_inc(w_ready, 1)

            def cond_lo(t):
                for h in range(KH):
                    dve.wait_ge(xc_hi_made, KH * t + h + 1)
                    nc.vector.tensor_tensor(xc_lo[:, h], front_bank(t, f"cond{h}"), f32(xc_hi[:, h]),
                                            ALU.subtract).then_inc(front_freed, 1)

            def phi_sum(t, s):
                dve.wait_ge(phi_parts, 4 * t + s + 1)
                nc.vector.scalar_tensor_tensor(phi[:, s], expo[:, s % 2], 1.0, phi[:, s],
                                               ALU.min, ALU.add).then_inc(phi_made, 1)

            def kv_scan(t, d):
                dve.wait_ge(phi_made, 4 * t + 2 * d + 1)
                nc.vector.tensor_tensor_scan(kcs[:, d], carry[:], phi[:, 2 * d], 0.0,
                                             ALU.mult, ALU.add).then_inc(attn_step[d], 1)
                dve.wait_ge(front_made, made(t, f"v{d}"))
                nc.vector.tensor_tensor(kvs[:, d], phi[:, 2 * d], front_bank(t, f"v{d}"),
                                        ALU.mult).then_inc(front_freed, 1)
                dve.wait_ge(front_freed, freed(t, f"v{d}"))
                nc.vector.tensor_tensor_scan(kvs[:, d], carry[:], kvs[:, d], 0.0,
                                             ALU.mult, ALU.add).then_inc(attn_step[d], 1)

            def ratio_terms(t, d):
                dve.wait_ge(phi_made, 4 * t + 2 * d + 2)
                dve.wait_ge(attn_step[d], STEPS * t + 1)
                nc.vector.tensor_tensor(kcs[:, d], phi[:, 2 * d + 1], kcs[:, d], ALU.mult).then_inc(attn_step[d], 1)
                dve.wait_ge(attn_step[d], STEPS * t + 2)
                nc.vector.tensor_tensor(kvs[:, d], phi[:, 2 * d + 1], kvs[:, d], ALU.mult).then_inc(attn_step[d], 1)

            def ratio(t, d):
                dve.wait_ge(guess_made, KH * t + d + 1)
                nc.vector.scalar_tensor_tensor(kcs[:, d], kcs[:, d], ATTN_EPS, guess[:, d],
                                               ALU.add, ALU.mult).then_inc(attn_step[d], 1)
                dve.wait_ge(attn_step[d], STEPS * t + 4)
                nc.vector.tensor_tensor(kvs[:, d], kvs[:, d], guess[:, d], ALU.mult).then_inc(attn_step[d], 1)
                dve.wait_ge(attn_step[d], STEPS * t + 6)
                nc.vector.scalar_tensor_tensor(kvs[:, d], kcs[:, d], 2.0, kvs[:, d],
                                               ALU.subtract, ALU.mult).then_inc(at_made, 1)

            def attn_lo(t, d):
                dve.wait_ge(at_hi_made, KH * t + d + 1)
                nc.vector.tensor_tensor(xc_lo[:, d], kvs[:, d], f32(xc_hi[:, d]), ALU.subtract).then_inc(at_ready, 1)

            def residual(t, h):
                dve.wait_ge(xcol_in, 16 * (t + 1))
                dve.wait_ge(front_made, made(t, f"out{h}"))
                if not is_first(t):
                    dve.wait_ge(held, t)
                nc.vector.scalar_tensor_tensor(x1[:, h], front_bank(t, f"out{h}"), -HEAD_SCALE, xcol[:, h],
                                               ALU.mult, ALU.add).then_inc(front_freed, 1)

            def x1_lo_part(t, h):
                dve.wait_ge(x1_hi_made, KH * t + h + 1)
                nc.vector.tensor_tensor(x1_lo[:, h], x1[:, h], f32(x1_hi[:, h]), ALU.subtract).then_inc(x1_ready, 1)

            def mask_lora(t):
                if is_first(t):
                    dve.wait_ge(mask_ready, 1)
                dve.wait_ge(front_made, made(t, "xa"))
                own = lmask[:, bass.ds(t * BPT, BPT)].unsqueeze(2).to_broadcast([P, BPT, C])
                nc.vector.tensor_tensor(xa[:].rearrange("p (b l) -> p b l", l=C),
                                        front_bank(t, "xa").rearrange("p (b l) -> p b l", l=C),
                                        own, ALU.mult).then_inc(front_freed, 1)

            def xa_lo_part(t):
                dve.wait_ge(xa_hi_made, t + 1)
                nc.vector.tensor_tensor(xa_lo[:], xa[:], f32(xa_hi[:]), ALU.subtract).then_inc(xa_ready, 1)

            def h2_lo_part(t, h):
                dve.wait_ge(h2_hi_made, KH * t + h + 1)
                nc.vector.tensor_tensor(h2_lo[:, h], front_bank(t, f"ada{h}"), f32(h2_hi[:, h]),
                                        ALU.subtract).then_inc(front_freed, 1)

            def hidden(i, b, first=False):
                m, j = divmod(b, MEMB)
                if not first and j % 2 == 0:
                    dve.wait_ge(sparse_ready, NB * (i - 1) + MEMB * m + j + 2)
                dve.wait_ge(silu_made, NB * i + b + 1)
                dve.wait_ge(gu_made, 2 * (NB * i + b) + 2)
                nc.vector.tensor_tensor(hid[:, m, j], silu[:, b % 2], up_ps[b % 2][:], ALU.mult).then_inc(hid_made, 1)

            SEL = 9

            def select_compare(i, m):
                base = SEL * (QB * i + m)
                dve.wait_ge(mag_made, NB * i + MEMB * (m + 1))
                if not (is_first(i) and m == 0):
                    dve.wait_ge(sparse_made, NB * i + MEMB * m)
                pairs = mag[:, m].rearrange("p (a b) n -> p a b n", b=2)
                nc.vector.tensor_tensor(inner[:], pairs[:, :, 0], pairs[:, :, 1], ALU.is_ge).then_inc(sel_step, 1)
                nc.vector.tensor_tensor(beats[:, 0], mag[:, m, 0:2], mag[:, m, 2:4], ALU.is_ge).then_inc(sel_step, 1)
                nc.vector.tensor_tensor(beats[:, 1, 0], mag[:, m, 0], mag[:, m, 3], ALU.is_ge).then_inc(sel_step, 1)
                nc.vector.tensor_tensor(beats[:, 1, 1], mag[:, m, 1], mag[:, m, 2], ALU.is_ge).then_inc(sel_step, 1)
                return base

            def select_count(i, m):
                base = SEL * (QB * i + m)
                dve.wait_ge(sel_step, base + 1)
                nc.vector.tensor_scalar(inner[:], inner[:], 3.0, None, ALU.mult).then_inc(sel_step, 1)
                dve.wait_ge(sel_step, base + 4)
                nc.vector.tensor_tensor(beats[:, 0], beats[:, 0], beats[:, 1], ALU.add).then_inc(sel_step, 1)
                dve.wait_ge(sel_step, base + 6)
                nc.vector.tensor_tensor(wins[:], beats[:, 0, 0], beats[:, 0, 1], ALU.add).then_inc(sel_step, 1)

            def select_rank(i, m):
                base = SEL * (QB * i + m)
                both = wins[:].unsqueeze(1).to_broadcast([P, 2, NT])
                dve.wait_ge(sel_step, base + 7)
                nc.vector.tensor_tensor(beats[:, 0], both, inner[:], ALU.add).then_inc(sel_step, 1)
                nc.vector.tensor_tensor(beats[:, 1], both, inner[:], ALU.subtract).then_inc(sel_step, 1)

            def select_keep(i, m):
                base = SEL * (QB * i + m)
                dve.wait_ge(sel_step, base + 9)
                for j, (rank, bound, op) in enumerate([
                        (beats[:, 0, 0], 4.0, ALU.is_ge), (beats[:, 1, 0], 1.0, ALU.is_ge),
                        (beats[:, 1, 1], 0.0, ALU.is_le), (beats[:, 0, 1], 3.0, ALU.is_le)]):
                    nc.vector.scalar_tensor_tensor(hid[:, m, j], rank, bound, hid[:, m, j],
                                                   op, ALU.mult).then_inc(sparse_made, 1)

            def sparse_lo_part(i, m, a):
                dve.wait_ge(sparse_hi_made, 2 * (QB * i + m) + a + 1)
                nc.vector.tensor_tensor(sparse_lo[:, 2 * a:2 * (a + 1)], hid[:, m, 2 * a:2 * (a + 1)],
                                        f32(sparse_hi[:, 2 * a:2 * (a + 1)]), ALU.subtract).then_inc(sparse_ready, 2)

            def result(i, last=False):
                for h in range(KH):
                    dve.wait_ge(down_made, NB * (i + 1))
                    dve.wait_ge(held, i + 1)
                    if last and not h:
                        dve.wait_ge(y_stored, 16 * i)
                    nc.vector.tensor_tensor(y[:, h], down_ps[h][:], x1_held[:, h], ALU.add).then_inc(y_made, 1)

            def step(i, first=False, last=False):
                t = i + 1
                if not first:
                    select_compare(i - 1, 1)
                    select_count(i - 1, 1)
                if not last:
                    cond_lo(t)
                if not first:
                    select_rank(i - 1, 1)
                hidden(i, 0, first)
                if not first:
                    select_keep(i - 1, 1)
                if not last:
                    phi_sum(t, 0)
                    phi_sum(t, 1)
                    phi_sum(t, 2)
                    kv_scan(t, 0)
                    phi_sum(t, 3)
                if not first:
                    sparse_lo_part(i - 1, 1, 0)
                if not last:
                    ratio_terms(t, 0)
                if not first:
                    sparse_lo_part(i - 1, 1, 1)
                hidden(i, 1, first)
                if not last:
                    kv_scan(t, 1)
                    ratio_terms(t, 1)
                if not first:
                    result(i - 1)
                if not last:
                    ratio(t, 0)
                    ratio(t, 1)
                hidden(i, 2, first)
                hidden(i, 3, first)
                if not last:
                    attn_lo(t, 0)
                    attn_lo(t, 1)
                select_compare(i, 0)
                hidden(i, 4, first)
                hidden(i, 5, first)
                if not last:
                    residual(t, 0)
                    residual(t, 1)
                    x1_lo_part(t, 0)
                    x1_lo_part(t, 1)
                select_count(i, 0)
                hidden(i, 6, first)
                if not last:
                    mask_lora(t)
                select_rank(i, 0)
                if not last:
                    xa_lo_part(t)
                select_keep(i, 0)
                sparse_lo_part(i, 0, 0)
                hidden(i, 7, first)
                if not last:
                    h2_lo_part(t, 0)
                sparse_lo_part(i, 0, 1)
                if not last:
                    h2_lo_part(t, 1)

            def adapter_masks():
                dve.wait_ge(tables_in, 48)
                nc.vector.tensor_scalar(lmask[:], aidx[:], lid[:], lscale[:], ALU.is_equal,
                                        ALU.mult).then_inc(mask_ready, 1)

            split_weight(0)
            split_weight(1)
            cond_lo(0)
            split_weight(2)
            split_weight(3)
            phi_sum(0, 0)
            dve.wait_ge(tables_ready, 3)
            kv_scan(0, 0)
            phi_sum(0, 1)
            adapter_masks()
            ratio_terms(0, 0)
            phi_sum(0, 2)
            kv_scan(0, 1)
            phi_sum(0, 3)
            ratio_terms(0, 1)
            split_weight(4)
            ratio(0, 0)
            ratio(0, 1)
            split_weight(5)
            attn_lo(0, 0)
            attn_lo(0, 1)
            split_weight(6)
            split_weight(7)
            residual(0, 0)
            residual(0, 1)
            x1_lo_part(0, 0)
            x1_lo_part(0, 1)
            split_weight(8)
            mask_lora(0)
            xa_lo_part(0)
            split_weight(9)
            h2_lo_part(0, 0)
            h2_lo_part(0, 1)
            split_weight(10)
            split_weight(11)
            step(0, first=True)
            with dve.Fori(1, TILES - 1) as i:
                step(i)
            step(TILES - 1, last=True)
            select_compare(TILES - 1, 1)
            select_count(TILES - 1, 1)
            select_rank(TILES - 1, 1)
            select_keep(TILES - 1, 1)
            for a in range(2):
                sparse_lo_part(TILES - 1, 1, a)
            result(TILES - 1, last=True)


def kernel(**inputs):
    import numpy as _np
    import concourse.bacc as _bacc
    from concourse.bass_utils import run_bass_kernel_spmd as _run

    g = {k: _np.asarray(v) for k, v in inputs.items()}
    x = g["x"]
    B, C, T = x.shape
    rows = x.reshape(B * C, T)
    NA, RANK, _ = g["L0_cond2_A"].shape
    S = g["L0_cond_weights"].shape[0]
    GATE = g["L0_ffn_w_gate"].shape

    def members(w):
        return w.reshape(GATE[0], GATE[1] // 4, 4).transpose(0, 2, 1)

    arrays = {
        "x_rows": rows,
        "x_cols": rows.T,
        "cond_idx": g["itok_B_1_198"].reshape(B, 1),
        "adapter_idx": g["itok_B_0_6"].reshape(1, B),
        "cond_w": g["L0_cond_weights"].reshape(S, C * C),
        "w_qkv": g["L0_attn_W_qkv"].T,
        "w_out": g["L0_attn_W_out"].T,
        "w_ada": g["L0_cond2_W"].T,
        "lora_a": g["L0_cond2_A"].reshape(NA * RANK, T).T,
        "lora_b": g["L0_cond2_Bm"].transpose(0, 2, 1).reshape(NA * RANK, T),
        "lora_scale": _np.repeat(g["L0_cond2_scalings"], RANK).reshape(NA * RANK, 1),
        "lora_id": _np.repeat(_np.arange(NA, dtype=_np.float32), RANK).reshape(NA * RANK, 1),
        "w_gate": members(g["L0_ffn_w_gate"]),
        "w_up": members(g["L0_ffn_w_up"]),
        "w_down": g["L0_ffn_w_down"].reshape(GATE[1] // 4, 4 * T),
    }
    nc = _bacc.Bacc("TRN2", target_bir_lowering=False, num_devices=1)
    arrays = {f"in_{k}": _np.ascontiguousarray(v) for k, v in arrays.items()}
    args = [nc.dram_tensor(k, v.shape, mybir.dt.from_np(v.dtype), kind="ExternalInput").ap()
            for k, v in arrays.items()]
    args.append(nc.dram_tensor("out_y", (T, B * C), F32, kind="ExternalOutput").ap())
    adaln_attn_ffn(nc, *args)
    r = _run(nc, [arrays], core_ids=[0])
    return r.results[0]["out_y"].T.reshape(B, C, T)
```
